# Optimizing a Trainium2 kernel written in Bass

```python
import numpy as np
import jax
import jax.numpy as jnp

def _softmax(x, axis=-1):
    return jax.nn.softmax(x, axis=axis)

def _gelu(x):
    return jax.nn.gelu(x, approximate=True)

def _silu(x):
    return jax.nn.silu(x)

def _sigmoid(x):
    return jax.nn.sigmoid(x)

def _layernorm(x, axis=-1, eps=1e-05):
    m = jnp.mean(x, axis=axis, keepdims=True)
    v = jnp.var(x, axis=axis, keepdims=True)
    return (x - m) / jnp.sqrt(v + eps)

def _scatter_add(tgt, idx, src, axis=0):
    return tgt.at[idx].add(src)

def _segment_sum(src, seg, n):
    return jax.ops.segment_sum(src, seg, n)
kernel_name = 'mk_gnn_ffn_d1_gnn_r8_2b20d7'

def setup_inputs(seed: int=0):
    np.random.seed(seed)
    _w = jnp.asarray

    def _rec_inputs():
        import jax
        import jax.numpy as jnp
        _gk = jax.random.key(seed)
        x = -0.0002117 + 1 * jax.random.normal(jax.random.fold_in(_gk, 1), (6250, 256), jnp.float32)
        src = jax.random.randint(jax.random.fold_in(_gk, 2), (200000,), 0, 6250, jnp.int32)
        dst = jnp.minimum((6250 * jax.random.uniform(jax.random.fold_in(_gk, 3), (200000,)) ** 2.0).astype(jnp.int32), 49999)
        _o = jnp.argsort(dst, stable=True)
        src = src[_o]
        dst = dst[_o]
        edge_weight = jax.random.uniform(jax.random.fold_in(_gk, 12), (200000,), jnp.float32, 0.0, 0.03125)
        return (x, src, dst, edge_weight)
    x, src, dst, edge_weight = _rec_inputs()

    def _L0_gnn_setup():
        import jax, jax.numpy as jnp
        import numpy as np
        N_NODES = 12500
        N_EDGES = 400000
        DIM = 256
        LEAKY_SLOPE = 0.2
        EPS = 1e-12
        key = jax.random.key(seed)
        ks = jax.random.split(key, 8)
        embeddings = jax.random.normal(ks[0], (N_NODES, DIM), dtype=jnp.float32)
        edge_src = jax.random.randint(ks[1], (N_EDGES,), 0, N_NODES, dtype=jnp.int32)
        edge_dst = jax.random.randint(ks[2], (N_EDGES,), 0, N_NODES, dtype=jnp.int32)
        edge_val = jax.random.uniform(ks[3], (N_EDGES,), dtype=jnp.float32) / 32.0
        scale = 1.0 / np.sqrt(DIM)
        W1 = jax.random.normal(ks[4], (DIM, DIM), dtype=jnp.float32) * scale
        b1 = jax.random.normal(ks[5], (DIM,), dtype=jnp.float32) * 0.01
        W2 = jax.random.normal(ks[6], (DIM, DIM), dtype=jnp.float32) * scale
        b2 = jax.random.normal(ks[7], (DIM,), dtype=jnp.float32) * 0.01
        return {'embeddings': embeddings, 'edge_src': edge_src, 'edge_dst': edge_dst, 'edge_val': edge_val, 'W1': W1, 'b1': b1, 'W2': W2, 'b2': b2}
    _L0_gnn_all = _L0_gnn_setup()
    _L0_gnn_in = {k: v for k, v in _L0_gnn_all.items() if k in ('W1', 'b1', 'W2', 'b2')}
    del _L0_gnn_all

    def _L0_ffn_setup():
        import jax, jax.numpy as jnp
        import numpy as np
        NUM_EXPERTS = 8
        TOP_K = 2
        B, S, D = (8, 1024, 256)

        def _moe(tokens, router_w, w1, b1, w2, b2):
            N = tokens.shape[0]
            E = router_w.shape[0]
            logits = tokens.astype(jnp.float32) @ router_w.astype(jnp.float32).T
            probs = jax.nn.softmax(logits, axis=-1)
            rw, re = jax.lax.top_k(probs, TOP_K)
            if TOP_K > 1:
                rw = rw / jnp.maximum(rw.sum(-1, keepdims=True), 1e-12)
            rw = rw.astype(tokens.dtype)
            combine = jnp.zeros((N, E), tokens.dtype).at[jnp.arange(N)[:, None], re].set(rw)
            out = tokens
            for e in range(E):
                h = jax.nn.gelu(tokens @ w1[e] + b1[e], approximate=False)
                y = h @ w2[e] + b2[e]
                out = out + combine[:, e:e + 1] * y
            return out
        key = jax.random.key(seed)
        ks = jax.random.split(key, 4)
        scale = 1.0 / np.sqrt(D).astype(np.float32)
        return {'input_embeddings': jax.random.normal(ks[0], (B, S, D), jnp.float32), 'router_w': jax.random.normal(ks[1], (NUM_EXPERTS, D), jnp.float32) * scale, 'w1': jax.random.normal(ks[2], (NUM_EXPERTS, D, D), jnp.float32) * scale, 'b1': jnp.zeros((NUM_EXPERTS, D), jnp.float32), 'w2': jax.random.normal(ks[3], (NUM_EXPERTS, D, D), jnp.float32) * scale, 'b2': jnp.zeros((NUM_EXPERTS, D), jnp.float32)}
    _L0_ffn_all = _L0_ffn_setup()
    _L0_ffn_in = {k: v for k, v in _L0_ffn_all.items() if k in ('router_w', 'w1', 'b1', 'w2', 'b2')}
    del _L0_ffn_all
    return {'x': x, 'src': src, 'dst': dst, 'edge_weight': edge_weight, 'L0_gnn_W1': _L0_gnn_in['W1'], 'L0_gnn_b1': _L0_gnn_in['b1'], 'L0_gnn_W2': _L0_gnn_in['W2'], 'L0_gnn_b2': _L0_gnn_in['b2'], 'L0_ffn_router_w': _L0_ffn_in['router_w'], 'L0_ffn_w1': _L0_ffn_in['w1'], 'L0_ffn_b1': _L0_ffn_in['b1'], 'L0_ffn_w2': _L0_ffn_in['w2'], 'L0_ffn_b2': _L0_ffn_in['b2']}

def reference(x, src, dst, edge_weight, L0_gnn_W1, L0_gnn_b1, L0_gnn_W2, L0_gnn_b2, L0_ffn_router_w, L0_ffn_w1, L0_ffn_b1, L0_ffn_w2, L0_ffn_b2):
    import jax
    import jax.numpy as jnp

    def _L0_gnn_ref(embeddings, edge_src, edge_dst, edge_val, W1, b1, W2, b2):
        import jax, jax.numpy as jnp
        import numpy as np
        N_NODES = 12500
        N_EDGES = 400000
        DIM = 256
        LEAKY_SLOPE = 0.2
        EPS = 1e-12
        ego_emb = embeddings @ W1.T + b1
        messages = edge_val[:, None] * embeddings[edge_src]
        neighbor_emb = jax.ops.segment_sum(messages, edge_dst, num_segments=embeddings.shape[0])
        interaction_emb = neighbor_emb * embeddings
        side_emb = (neighbor_emb + interaction_emb) @ W2.T + b2
        out = ego_emb + side_emb
        out = jnp.where(out >= 0, out, LEAKY_SLOPE * out)
        norm = jnp.sqrt(jnp.sum(out * out, axis=1, keepdims=True))
        return out / jnp.maximum(norm, EPS)

    def _L0_ffn_ref(input_embeddings, router_w, w1, b1, w2, b2):
        import jax, jax.numpy as jnp
        import numpy as np
        NUM_EXPERTS = 8
        TOP_K = 2
        B, S, D = (8, 1024, 256)

        def _moe(tokens, router_w, w1, b1, w2, b2):
            N = tokens.shape[0]
            E = router_w.shape[0]
            logits = tokens.astype(jnp.float32) @ router_w.astype(jnp.float32).T
            probs = jax.nn.softmax(logits, axis=-1)
            rw, re = jax.lax.top_k(probs, TOP_K)
            if TOP_K > 1:
                rw = rw / jnp.maximum(rw.sum(-1, keepdims=True), 1e-12)
            rw = rw.astype(tokens.dtype)
            combine = jnp.zeros((N, E), tokens.dtype).at[jnp.arange(N)[:, None], re].set(rw)
            out = tokens
            for e in range(E):
                h = jax.nn.gelu(tokens @ w1[e] + b1[e], approximate=False)
                y = h @ w2[e] + b2[e]
                out = out + combine[:, e:e + 1] * y
            return out
        b, s, d = input_embeddings.shape
        tokens = input_embeddings.reshape(b * s, d)
        return _moe(tokens, router_w, w1, b1, w2, b2).reshape(b, s, d)
    x = x + _L0_gnn_ref(_layernorm(x, axis=-1), src, dst, edge_weight, L0_gnn_W1, L0_gnn_b1, L0_gnn_W2, L0_gnn_b2)
    x = x + _L0_ffn_ref(_layernorm(x, axis=-1)[None], L0_ffn_router_w, L0_ffn_w1, L0_ffn_b1, L0_ffn_w2, L0_ffn_b2)[0]
    return x

_drawn_inputs = setup_inputs


def setup_inputs(seed=0):
    import zlib

    import numpy as np

    out = dict(_drawn_inputs(seed))
    spreads = {'L0_ffn_b1': (0.0, 0.325), 'L0_ffn_b2': (0.0, 0.1)}
    factors = {'edge_weight': 5.217, 'L0_gnn_b1': 52.429, 'L0_gnn_W2': 3.381, 'L0_gnn_b2': 64.0}
    for name, (base, spread) in spreads.items():
        noise = np.random.default_rng([zlib.crc32(name.encode()), seed]).standard_normal(out[name].shape)
        drawn = base * np.exp(spread * noise) if base else spread * noise
        out[name] = jnp.asarray(drawn.astype(out[name].dtype))
    for name, factor in factors.items():
        out[name] = (out[name] * factor).astype(out[name].dtype)
    return out
```

```python
import numpy as np
import concourse.bass as bass
from concourse import mybir
from contextlib import ExitStack

P = 128
QUAD = 4
RING = 32
HALF = RING // 2
LN_EPS = 1e-5
NORM_EPS = 1e-12
LEAKY_SLOPE = 0.2
NO_NODE = float(1 << 20)
TABLE = 4


def ceil_div(a, b):
    return -(-a // b)


def gnn_ffn_kernel(nc, x, src, dst, edge_weight, gnn_w1, gnn_b1, gnn_w2, gnn_b2,
                   router_w, ffn_w1, ffn_b1, ffn_w2, ffn_b2, out):
    fp32, bf16, i32, u32 = mybir.dt.float32, mybir.dt.bfloat16, mybir.dt.int32, mybir.dt.uint32
    ALU = mybir.AluOpType
    ACT = mybir.ActivationFunctionType
    AX = mybir.AxisListType.X

    N, D = x.shape
    E = src.shape[0]
    NE = router_w.shape[0]
    DC = D // P
    NB = ceil_div(N, P)
    LAST = N - (NB - 1) * P
    TILES = ceil_div(ceil_div(E, P), RING) * RING
    NQ = TILES // QUAD
    CHUNKS = TILES // RING
    RQ = RING // QUAD
    QP = P // QUAD
    MB = ceil_div(TILES, P)
    FULL = E // P
    FB = FULL // P
    FR = FULL - FB * P
    FT = E - FULL * P
    PACKS = ceil_div(MB, 4)
    PACK_ORDER = (1, 0, 2)
    AHEAD = 3
    BACK = RQ - AHEAD
    NVIS = 3

    J = N // P
    JG = 8
    groups = [(j, min(JG, J - j)) for j in range(0, J, JG)]
    NM = J * P
    NR = N - NM
    NG = len(groups)
    NLN = NG + (NR > 0)

    ctx = ExitStack()
    with ctx:
        def sb(name, shape, dt=fp32):
            return ctx.enter_context(nc.sbuf_tensor(name, shape, dt))

        def sem(name):
            return ctx.enter_context(nc.semaphore(name))

        xn_dram = nc.dram_tensor("xn_scratch", (N, D), fp32).ap()
        quad_dram = nc.dram_tensor("quad_scratch", (2, MB * QP), fp32).ap()
        table_dram = nc.dram_tensor("table_scratch", (NB, TABLE), i32).ap()

        ident = sb("ident", [P, P])
        iota_row_i = sb("iota_row_i", [P, P], i32)
        iota_row = sb("iota_row", [P, P])
        zero_row = sb("zero_row", [1, D], bf16)
        base_i = sb("base_i", [P, 1], i32)
        base = sb("base", [P, 1])
        ones_col = sb("ones_col", [P, 1])
        before = sb("before", [NB, NB])
        quad_no_i = sb("quad_no_i", [NB, NQ], i32)
        quad_no = sb("quad_no", [NB, NQ])
        w_raw = sb("w_raw", [P, 2, DC, D])
        w_gnn = sb("w_gnn", [P, 2, DC, D])
        bias_gnn = sb("bias_gnn", [P, 2, D])
        router_raw = sb("router_raw", [NE, D])
        router_t = sb("router_t", [P, DC, NE])
        b1_raw = sb("b1_raw", [NE * DC, P])
        b1_t = sb("b1_t", [P, NE * DC])
        b2_sb = sb("b2_sb", [NE, D])

        edge_int = sb("edge_int", [P, 2, MB * P], i32)
        edge_raw = sb("edge_raw", [P, 3, MB * P])
        src_t = sb("src_t", [P, MB * P], i32)
        dst_t = sb("dst_t", [P, MB * P])
        wgt_t = sb("wgt_t", [P, MB * P])
        tile_lim = sb("tile_lim", [P, 2, MB])
        quad_lim = sb("quad_lim", [MB, 2, QP])
        quad_all = sb("quad_all", [NB, 2, MB * QP])
        scratch_q = sb("scratch_q", [NB, NQ])
        tab = sb("tab", [NB, 12])
        table_i = sb("table_i", [NB, TABLE], i32)
        table = sb("table", [1, NB * TABLE], i32)
        released = sb("released", [1, NQ], i32)

        WN = NE * DC * D
        start_buf = sb("start_buf", [P, max(J * D, 2 * WN)])
        x_all = start_buf[:, 0:J * D]
        w1_sb = start_buf[:, 0:WN].rearrange("p (e c h) -> p e c h", e=NE, c=DC)
        w2_sb = start_buf[:, WN:2 * WN].rearrange("p (e c h) -> p e c h", e=NE, c=DC)
        x_rest = sb("x_rest", [P, D])
        stats = sb("stats", [P, (J + 1) * 6])
        mean_var = sb("mean_var", [P, (J + 1) * 2])
        var_eps = sb("var_eps", [P, J + 1])
        std = sb("std", [P, J + 1])
        rstd_all = sb("rstd_all", [P, J + 1])
        shift_all = sb("shift_all", [P, J + 1])

        index = [sb(f"index{h}", [P, HALF], i32) for h in range(2)]
        ring = sb("ring", [P, RING * D])
        onehot = [sb(f"onehot{k}", [P, P]) for k in range(QUAD)]
        iota_block = sb("iota_block", [P, P])

        x_blk = sb("x_blk", [P, D])
        xn_blk = sb("xn_blk", [P, D])
        xn_t = sb("xn_t", [P, DC * P])
        mixed = sb("mixed", [P, D])
        mixed_t = sb("mixed_t", [P, DC * P])
        pre = sb("pre", [P, D])
        act = sb("act", [P, D])
        junk = sb("junk", [P, D])
        x1 = sb("x1", [P, D])
        tokens = sb("tokens", [P, D])
        tokens_t = sb("tokens_t", [P, DC, P])
        resid = sb("resid", [P, D])
        st2 = sb("st2", [P, 6])
        mv2 = sb("mv2", [P, 2])
        sumsq = sb("sumsq", [P, 1])
        newton = [sb(f"newton{n}", [P, 8]) for n in range(2)]
        logit_max = sb("logit_max", [P, 1])
        exps = sb("exps", [P, NE])
        exp_sum = sb("exp_sum", [P, 1])
        exp_rec = sb("exp_rec", [P, 1])
        probs = sb("probs", [P, NE])
        top = sb("top", [P, 8])
        top_at = sb("top_at", [P, 8], u32)
        top_f = sb("top_f", [P, 2])
        den = sb("den", [P, 1])
        den_rec = sb("den_rec", [P, 1])
        mask1 = sb("mask1", [P, NE])
        mask2 = sb("mask2", [P, NE])
        combine = sb("combine", [P, NE])
        combine_t = sb("combine_t", [NE, P])
        hidden = [sb(f"hidden{n}", [P, DC, P]) for n in range(2)]
        acc = sb("acc", [P, D])
        out_blk = sb("out_blk", [P, D])

        bank = [ctx.enter_context(nc.psum_tensor(f"bank{n}", [P, 512], fp32)) for n in range(8)]
        neigh_ps = bank[0][:, 0:D]
        xn_t_ps, mixed_t_ps = bank[1][:, 0:DC * P], bank[1][:, DC * P:2 * DC * P]
        dense_ps = bank[2][:, 0:D]
        b2_ps = bank[2][:, D:2 * D]
        tokens_t_ps = bank[3][:, 0:DC * P]
        logits_ps = bank[3][:, DC * P:DC * P + NE]
        combine_t_ps = bank[3][0:NE, DC * P + P:DC * P + 2 * P]
        hidden_ps = [bank[4 + n][:, 0:DC * P] for n in range(2)]
        y_ps = [bank[6 + n][:, 0:D] for n in range(2)]

        s_edge = [sem(f"edge{a}_in") for a in range(3)]
        EDGE_IN = 16 * ((FB > 0) + (FR > 0) + (FT > 0))
        s_x = [sem(f"x_in{g}") for g in range(NG + 1)]
        s_wgnn, s_small, s_ffn = sem("gnn_weights_in"), sem("small_in"), sem("ffn_weights_in")
        fill_done = sem("fill_done")
        const_chain = sem("const_chain")
        consts_done = sem("consts_done")
        float_done = [sem(f"float_done{a}") for a in range(2)]
        lim_done = sem("tile_limits")
        lim_t_done = sem("tile_limits_t")
        quad_lim_done = sem("quad_limits")
        quad_out, quad_back = sem("quad_limits_out"), sem("quad_limits_back")
        nv_done = sem("visits")
        vbase_psd = sem("visits_before")
        released_parts, released_psd, released_done = sem("released_parts"), sem("released_ps"), sem("released_done")
        table_done, table_out, table_in = sem("table_done"), sem("table_out"), sem("table_in")
        edge_t_psd = [sem(f"edge_t_ps{a}") for a in range(3)]
        edge_t_done = [sem(f"edge_t{a}") for a in range(3)]
        gnn_t_psd, gnn_t_done = sem("gnn_t_ps"), sem("gnn_t_done")
        small_t_psd, small_t_done = sem("small_t_ps"), sem("small_t_done")
        stats_done, aggr_done, var_done, std_done, scale_done, xn_done = (
            sem("ln_stats"), sem("ln_aggr"), sem("ln_var"), sem("ln_std"), sem("ln_scale"), sem("ln_rows"))
        xn_out = sem("xn_out")
        dve_chain = sem("dve_chain")

        index_ready = [sem(f"index_ready{h}") for h in range(2)]
        index_read = [sem(f"index_read{h}") for h in range(2)]
        landed = [sem(f"landed{q}") for q in range(RQ)]
        quads_landed = sem("quads_landed")
        quads_free = sem("quads_free")
        quads_begun = sem("quads_begun")
        onehot_ready = [sem(f"onehot_ready{k}") for k in range(QUAD)]
        onehot_used = [sem(f"onehot_used{k}") for k in range(QUAD)]

        x_loaded = sem("x_loaded")
        x_used = sem("x_used")
        iota_ready = sem("iota_ready")
        neigh_done = sem("neigh_done")
        xn_t_psd, xn_t_done = sem("xn_t_ps"), sem("xn_t_done")
        mixed_done = sem("mixed_done")
        mixed_t_psd, mixed_t_done = sem("mixed_t_ps"), sem("mixed_t_done")
        dense_done = sem("dense_done")
        tokens_done = sem("tokens_done")
        tokens_t_psd, tokens_t_done = sem("tokens_t_ps"), sem("tokens_t_done")
        logits_done = sem("logits_done")
        max_done = sem("max_done")
        exp_done = sem("exp_done")
        combine_done = sem("combine_done")
        gnn_chain = sem("gnn_chain")
        ct_psd, ct_done, b2_done = sem("combine_t_ps"), sem("combine_t_done"), sem("b2_done")
        h_psd = [sem(f"hidden_ps{e}") for e in range(NE)]
        h_done = [sem(f"hidden_done{e}") for e in range(NE)]
        y_done = [sem(f"y_done{e}") for e in range(NE)]
        acc_done = [sem(f"acc_done{e}") for e in range(NE)]
        out_ready = sem("out_ready")
        out_stored = sem("out_stored")

        block = ctx.enter_context(nc.Block())

        @block.sync
        def _(sp):
            sp.wait_ge(fill_done, 3)

            def edge_load(dram, buf, s):
                if FB:
                    sp.dma_start(buf[:, 0:FB * P].rearrange("p (m f) -> p m f", f=P),
                                 dram[0:FB * P * P].rearrange("(m p f) -> p m f", p=P, f=P)).then_inc(s, 16)
                if FR:
                    sp.dma_start(buf[0:FR, FB * P:FB * P + P],
                                 dram[FB * P * P:FULL * P].rearrange("(p f) -> p f", f=P)).then_inc(s, 16)
                if FT:
                    sp.dma_start(buf[FR:FR + 1, FB * P:FB * P + FT],
                                 dram[FULL * P:E].rearrange("(p f) -> p f", p=1)).then_inc(s, 16)

            edge_load(dst, edge_int[:, 1, :], s_edge[1])
            x_main = x[0:NM, :].rearrange("(p j) d -> p (j d)", p=P)
            xn_main = xn_dram[0:NM, :].rearrange("(p j) d -> p (j d)", p=P)
            edge_load(src, edge_int[:, 0, :], s_edge[0])
            for g, (j, n) in enumerate(groups):
                sp.dma_start(x_all[:, j * D:(j + n) * D], x_main[:, j * D:(j + n) * D]).then_inc(s_x[g], 16)
                if g == min(1, NG - 1):
                    edge_load(edge_weight, edge_raw[:, 2, :], s_edge[2])
            if NR:
                sp.wait_ge(dve_chain, 1)
                sp.dma_start(x_rest[0:NR, :], x[NM:N, :]).then_inc(s_x[NG], 16)
            sp.wait_ge(quad_lim_done, 2)
            sp.dma_start(quad_dram.rearrange("a (m q) -> m a q", q=QP), quad_lim[:, :, :]).then_inc(quad_out, 16)
            sp.wait_ge(quad_out, 16)
            sp.dma_start(quad_all[:, :, :], quad_dram.partition_broadcast(NB)).then_inc(quad_back, 16)
            for g, (j, n) in enumerate(groups):
                sp.wait_ge(xn_done, min(J, j + n))
                sp.dma_start(xn_main[:, j * D:(j + n) * D], x_all[:, j * D:(j + n) * D]).then_inc(xn_out, 16)
            if NR:
                sp.wait_ge(xn_done, J + 1)
                sp.dma_start(xn_dram[NM:N, :], x_rest[0:NR, :]).then_inc(xn_out, 16)
            sp.wait_ge(table_done, 1)
            sp.dma_start(table_dram, table_i[:, :]).then_inc(table_out, 16)
            sp.wait_ge(table_out, 16)
            sp.dma_start(table[:, :], table_dram.rearrange("b t -> (b t)").rearrange("(a n) -> a n", a=1))\
                .then_inc(table_in, 16)
            sp.wait_ge(xn_out, 16 * NLN)
            sp.dma_start(w1_sb[:, :, :, :], ffn_w1.rearrange("e (c p) h -> p e c h", p=P)).then_inc(s_ffn, 16)
            sp.dma_start(w2_sb[:, :, :, :], ffn_w2.rearrange("e (c p) h -> p e c h", p=P)).then_inc(s_ffn, 16)

            sp.wait_ge(table_in, 16)
            sp.wait_ge(released_done, 1)
            sp.sem_inc(quads_free, AHEAD)
            passes = sp.value_load(table[0:1, 3:4], min_val=1, max_val=NB)
            with sp.Fori(0, passes) as turn:
                with sp.Fori(0, CHUNKS) as c:
                    count = sp.snap((turn * CHUNKS + c + 1) * (16 * QUAD))
                    for q in range(RQ):
                        sp.wait_ge(landed[q], count)
                        sp.sem_inc(quads_landed, 1)
                        used = sp.value_load(released[0:1, bass.ds(c * RQ + q, 1)], min_val=1, max_val=NB * NQ)
                        sp.wait_ge(onehot_used[QUAD - 1], used + turn * NQ)
                        sp.sem_inc(quads_free, 1)

        @block.gpsimd
        def _(pool):
            gp = nc.gpsimd
            gp.memset(edge_int[:, 1, FB * P:MB * P], int(NO_NODE)).then_inc(fill_done, 1)
            gp.memset(edge_int[:, 0, FB * P:MB * P], 0).then_inc(fill_done, 1)
            gp.memset(edge_raw[:, 2, FB * P:MB * P], 0.0).then_inc(fill_done, 1)
            gp.memset(ident[:, :], 0.0).then_inc(const_chain, 1)
            gp.memset(before[:, :], 1.0).then_inc(const_chain, 1)
            gp.iota(iota_row_i[:, :], [[1, P]], base=0, channel_multiplier=0).then_inc(const_chain, 1)
            gp.iota(base_i[:, :], [[0, 1]], base=0, channel_multiplier=P).then_inc(const_chain, 1)
            gp.iota(quad_no_i[:, :], [[1, NQ]], base=1, channel_multiplier=0).then_inc(const_chain, 1)
            gp.memset(zero_row[:, :], 0.0).then_inc(consts_done, 1)
            gp.memset(ones_col[:, :], 1.0).then_inc(consts_done, 1)
            pool.wait_ge(const_chain, 5)
            gp.affine_select(out=ident[:, :], in_=ident[:, :], compare_op=ALU.not_equal, fill=1.0,
                             base=0, pattern=[[-1, P]], channel_multiplier=1).then_inc(consts_done, 1)
            gp.affine_select(out=before[:, :], in_=before[:, :], compare_op=ALU.is_gt, fill=0.0,
                             base=0, pattern=[[1, NB]], channel_multiplier=-1).then_inc(consts_done, 1)
            gp.tensor_copy(iota_row[:, :], iota_row_i[:, :]).then_inc(consts_done, 1)
            gp.tensor_copy(base[:, :], base_i[:, :]).then_inc(consts_done, 1)
            gp.tensor_copy(quad_no[:, :], quad_no_i[:, :]).then_inc(consts_done, 1)

            pool.wait_ge(edge_t_done[0], PACKS)
            pool.wait_ge(table_in, 16)
            pool.wait_ge(xn_out, 16 * NLN)
            passes = pool.value_load(table[0:1, 3:4], min_val=1, max_val=NB)
            for h in range(2):
                pool.sem_inc(index_read[h], 1)
            with pool.Fori(0, passes) as turn:
                with pool.Fori(0, CHUNKS) as c:
                    lap = pool.snap(turn * CHUNKS + c + 1)
                    free = pool.snap((turn * CHUNKS + c) * RQ + 1)
                    for h in range(2):
                        pool.wait_ge(index_read[h], lap)
                        gp.tensor_copy(index[h][:, :], src_t[:, bass.ds(c * RING + h * HALF, HALF)])\
                            .then_inc(index_ready[h], 1)
                        pool.wait_ge(index_ready[h], lap)
                        for i in range(HALF):
                            r = h * HALF + i
                            if r % QUAD == 0:
                                pool.wait_ge(quads_free, free + r // QUAD)
                                pool.sem_inc(quads_begun, 1)
                            gp.indirect_dma_start(
                                out=ring[:, r * D:(r + 1) * D], out_offset=None, in_=xn_dram[:, :],
                                in_offset=bass.IndirectOffsetOnAxis(ap=index[h][:, i:i + 1], axis=0),
                                engine_sem=index_read[h] if i == HALF - 1 else None,
                            ).then_inc(landed[r // QUAD], 16)

        @block.tensor
        def _(pe):
            mm, tr = nc.tensor.matmul, nc.tensor.transpose
            pe.wait_ge(consts_done, 7)

            def edge_packs(a):
                for n, m0 in enumerate(range(0, MB, 4)):
                    no = PACK_ORDER.index(a) * PACKS + n
                    if no >= 4:
                        prev = PACK_ORDER[(no - 4) // PACKS]
                        pe.wait_ge(edge_t_done[prev], (no - 4) % PACKS + 1)
                    for m in range(m0, min(MB, m0 + 4)):
                        last = tr(bank[4 + no % 4][:, (m - m0) * P:(m - m0 + 1) * P],
                                  edge_raw[:, a, m * P:(m + 1) * P], ident[:, :])
                    last.then_inc(edge_t_psd[a], 1)

            pe.wait_ge(lim_done, 2)
            for a in range(2):
                last = tr(bank[0][0:MB, a * P:(a + 1) * P], tile_lim[:, a, :], ident[:, :])
            last.then_inc(lim_t_done, 1)
            pe.wait_ge(float_done[1], 1)
            edge_packs(1)
            pe.wait_ge(float_done[0], 1)
            edge_packs(0)
            pe.wait_ge(s_edge[2], EDGE_IN)
            edge_packs(2)
            pe.wait_ge(nv_done, 1)
            mm(bank[0][0:NB, 256:257], before[:, :], tab[:, NVIS:NVIS + 1], start=True, stop=True)\
                .then_inc(vbase_psd, 1)
            pe.wait_ge(released_parts, 1)
            mm(bank[3][0:1, 0:NQ], ones_col[0:NB, :], scratch_q[:, :], start=True, stop=True)\
                .then_inc(released_psd, 1)
            pe.wait_ge(s_wgnn, 32)
            for n in range(2):
                for ic in range(DC):
                    for oc in range(DC):
                        last = tr(bank[1 + n][:, ic * D + oc * P:ic * D + (oc + 1) * P],
                                  w_raw[:, n, oc, ic * P:(ic + 1) * P], ident[:, :])
                last.then_inc(gnn_t_psd, 1)
            pe.wait_ge(s_small, 80)
            pe.wait_ge(released_done, 1)
            for c in range(DC):
                tr(bank[3][:, c * NE:(c + 1) * NE], router_raw[:, c * P:(c + 1) * P], ident[0:NE, 0:NE])
            tr(bank[3][:, DC * NE:DC * NE + NE * DC], b1_raw[:, :], ident[0:NE * DC, 0:NE * DC])\
                .then_inc(small_t_psd, 1)
            pe.wait_ge(edge_t_done[2], PACKS)
            pe.wait_ge(gnn_t_done, 2)
            pe.wait_ge(table_in, 16)
            for k in range(QUAD):
                pe.sem_inc(onehot_used[k], 1)

            def edges(b):
                lo = pe.value_load(table[0:1, bass.ds(b * TABLE, 1)], min_val=0, max_val=NB * NQ - 1)
                hi = pe.value_load(table[0:1, bass.ds(b * TABLE + 1, 1)], min_val=1, max_val=NB * NQ)
                visits = pe.value_load(table[0:1, bass.ds(b * TABLE + 2, 1)], min_val=0, max_val=NB * NQ)
                mm(neigh_ps, zero_row[:, 0:P], zero_row[:, 0:D], start=True, stop=False)
                with pe.Fori(lo, hi) as g:
                    at = pe.snap((g % RQ) * (QUAD * D))
                    visit = pe.snap(g + visits + 1)
                    pe.wait_ge(quads_landed, g + 1)
                    for k in range(QUAD):
                        pe.wait_ge(onehot_ready[k], visit)
                        mm(neigh_ps, onehot[k][:, :], ring[:, bass.ds(at + k * D, D)],
                           start=False, stop=False).then_inc(onehot_used[k], 1)
                mm(neigh_ps, zero_row[:, 0:P], zero_row[:, 0:D], start=False, stop=True)\
                    .then_inc(neigh_done, 1)

            def turn(b, f):
                bn = None if b is None else pe.snap(b + 1) if not isinstance(b, int) else b + 1
                fn = None if f is None else pe.snap(f + 1) if not isinstance(f, int) else f + 1

                def hid(e):
                    if f is None:
                        return
                    if e >= 2:
                        pe.wait_ge(h_done[e - 2], fn)
                    for hc in range(DC):
                        for c in range(DC):
                            last = mm(hidden_ps[e % 2][:, hc * P:(hc + 1) * P],
                                      w1_sb[:, e, c, hc * P:(hc + 1) * P], tokens_t[:, c, :],
                                      start=(c == 0), stop=(c == DC - 1))
                    last.then_inc(h_psd[e], 1)

                def outp(e):
                    if f is None:
                        return
                    pe.wait_ge(h_done[e], fn)
                    if e >= 2:
                        pe.wait_ge(acc_done[e - 2], fn)
                    for hc in range(DC):
                        last = mm(y_ps[e % 2], hidden[e % 2][:, hc, :], w2_sb[:, e, hc, :],
                                  start=(hc == 0), stop=(hc == DC - 1))
                    last.then_inc(y_done[e], 1)

                if b is not None:
                    edges(b)
                    pe.wait_ge(x_loaded, bn * 32)
                    for c in range(DC):
                        last = tr(xn_t_ps[:, c * P:(c + 1) * P], xn_blk[:, c * P:(c + 1) * P], ident[:, :])
                    last.then_inc(xn_t_psd, 1)
                if f is not None:
                    pe.wait_ge(combine_done, fn)
                    tr(combine_t_ps, combine[:, :], ident[:, :]).then_inc(ct_psd, 1)
                hid(0)
                hid(1)
                outp(0)
                if f is not None:
                    pe.wait_ge(ct_done, fn)
                    mm(b2_ps, combine_t[:, :], b2_sb[:, :], start=True, stop=True).then_inc(b2_done, 1)
                if b is not None:
                    pe.wait_ge(xn_t_done, bn)
                    pe.wait_ge(mixed_done, bn)
                    for c in range(DC):
                        last = tr(mixed_t_ps[:, c * P:(c + 1) * P], mixed[:, c * P:(c + 1) * P], ident[:, :])
                    last.then_inc(mixed_t_psd, 1)
                hid(2)
                outp(1)
                hid(3)
                outp(2)
                if b is not None:
                    for c in range(DC):
                        mm(dense_ps, xn_t[:, c * P:(c + 1) * P], w_gnn[:, 0, c, :], start=(c == 0), stop=False)
                    pe.wait_ge(mixed_t_done, bn)
                    for c in range(DC):
                        last = mm(dense_ps, mixed_t[:, c * P:(c + 1) * P], w_gnn[:, 1, c, :],
                                  start=False, stop=(c == DC - 1))
                    last.then_inc(dense_done, 1)
                hid(4)
                outp(3)
                hid(5)
                outp(4)
                hid(6)
                outp(5)
                if b is not None:
                    pe.wait_ge(tokens_done, bn)
                    for c in range(DC):
                        last = tr(tokens_t_ps[:, c * P:(c + 1) * P], tokens[:, c * P:(c + 1) * P], ident[:, :])
                    last.then_inc(tokens_t_psd, 1)
                hid(7)
                outp(6)
                outp(7)
                if b is not None:
                    pe.wait_ge(tokens_t_done, bn)
                    for c in range(DC):
                        last = mm(logits_ps, tokens_t[:, c, :], router_t[:, c, :],
                                  start=(c == 0), stop=(c == DC - 1))
                    last.then_inc(logits_done, 1)

            turn(0, None)
            pe.wait_ge(s_ffn, 32)
            with pe.Fori(1, NB) as b:
                turn(b, b - 1)
            turn(None, NB - 1)

        @block.scalar
        def _(act_e):
            act = nc.scalar.activation
            act_e.dma_start(bias_gnn[:, 0, :], gnn_b1.partition_broadcast(P)).then_inc(s_small, 16)
            act_e.dma_start(bias_gnn[:, 1, :], gnn_b2.partition_broadcast(P)).then_inc(s_small, 16)
            act_e.dma_start(router_raw[:, :], router_w).then_inc(s_small, 16)
            act_e.dma_start(b1_raw[:, :], ffn_b1.rearrange("e (c p) -> (e c) p", p=P)).then_inc(s_small, 16)
            act_e.dma_start(b2_sb[:, :], ffn_b2).then_inc(s_small, 16)
            act_e.dma_start(w_raw[:, 0, :, :], gnn_w1.rearrange("(c p) d -> p c d", p=P)).then_inc(s_wgnn, 16)
            act_e.dma_start(w_raw[:, 1, :, :], gnn_w2.rearrange("(c p) d -> p c d", p=P)).then_inc(s_wgnn, 16)
            act_e.wait_ge(s_edge[0], EDGE_IN)
            act_e.wait_ge(fill_done, 3)
            act(edge_raw[:, 0, :], edge_int[:, 0, :], ACT.Copy).then_inc(float_done[0], 1)

            def copy_packs(a):
                to = (src_t, dst_t, wgt_t)[a]
                for n, m0 in enumerate(range(0, MB, 4)):
                    no = PACK_ORDER.index(a) * PACKS + n
                    w = (min(MB, m0 + 4) - m0) * P
                    act_e.wait_ge(edge_t_psd[a], n + 1)
                    act(to[:, m0 * P:m0 * P + w], bank[4 + no % 4][:, 0:w], ACT.Copy).then_inc(edge_t_done[a], 1)

            def normalise(g):
                j, n = (groups + [(J, 1)])[g]
                act_e.wait_ge(var_done, g + 1)
                act(std[:, j:j + n], var_eps[:, j:j + n], ACT.Sqrt).then_inc(std_done, 1)

            def scale_rows(g):
                act_e.wait_ge(scale_done, g + 1)
                if g < NG:
                    j, n = groups[g]
                    with act_e.Fori(j, j + n) as r:
                        act(x_all[:, bass.ds(r * D, D)], x_all[:, bass.ds(r * D, D)], ACT.Identity,
                            bias=shift_all[:, bass.ds(r, 1)], scale=rstd_all[:, bass.ds(r, 1)]).then_inc(xn_done, 1)
                else:
                    act(x_rest[:, :], x_rest[:, :], ACT.Identity, bias=shift_all[:, J:J + 1],
                        scale=rstd_all[:, J:J + 1]).then_inc(xn_done, 1)

            copies = [1, 0, 2]
            for g in range(NLN):
                normalise(g)
                if g < 3:
                    copy_packs(copies[g])
                if g >= 1:
                    scale_rows(g - 1)
            scale_rows(NLN - 1)
            for g in range(NLN, 3):
                copy_packs(copies[g])
            for n in range(2):
                act_e.wait_ge(gnn_t_psd, n + 1)
                act(w_gnn[:, n, :, :], bank[1 + n][:, :].rearrange("p (c d) -> p c d", c=DC), ACT.Copy)\
                    .then_inc(gnn_t_done, 1)
            act_e.wait_ge(small_t_psd, 1)
            act(router_t[:, :, :], bank[3][:, 0:DC * NE].rearrange("p (c e) -> p c e", c=DC), ACT.Copy)
            act(b1_t[:, :], bank[3][:, DC * NE:2 * DC * NE], ACT.Copy).then_inc(small_t_done, 1)
            act_e.wait_ge(xn_out, 16 * NLN)
            act_e.sem_inc(out_stored, 16)

            def load_block(b, rows):
                act_e.dma_start(x_blk[0:rows, :], x[bass.ds(b * P, rows), :]).then_inc(x_loaded, 16)
                act_e.dma_start(xn_blk[0:rows, :], xn_dram[bass.ds(b * P, rows), :]).then_inc(x_loaded, 16)

            def turn(b, f, rows=P, out_rows=P):
                bn = None if b is None else act_e.snap(b + 1) if not isinstance(b, int) else b + 1
                fn = None if f is None else act_e.snap(f + 1) if not isinstance(f, int) else f + 1

                def gelu(e):
                    if f is None:
                        return
                    act_e.wait_ge(h_psd[e], fn)
                    if e >= 2:
                        act_e.wait_ge(y_done[e - 2], fn)
                    for hc in range(DC):
                        last = act(hidden[e % 2][:, hc, :], hidden_ps[e % 2][:, hc * P:(hc + 1) * P], ACT.Gelu,
                                   bias=b1_t[:, e * DC + hc:e * DC + hc + 1])
                    last.then_inc(h_done[e], 1)

                if b is not None:
                    if f is not None:
                        act_e.wait_ge(x_used, fn)
                    load_block(b, rows)
                    act_e.wait_ge(xn_t_psd, bn)
                    act(xn_t[:, :], xn_t_ps, ACT.Copy).then_inc(xn_t_done, 1)
                if f is not None:
                    act_e.wait_ge(ct_psd, fn)
                    act(combine_t[:, :], combine_t_ps, ACT.Copy).then_inc(ct_done, 1)
                gelu(0)
                gelu(1)
                if b is not None:
                    act_e.wait_ge(mixed_t_psd, bn)
                    act(mixed_t[:, :], mixed_t_ps, ACT.Copy).then_inc(mixed_t_done, 1)
                for e in range(2, NE):
                    gelu(e)
                if b is not None:
                    act_e.wait_ge(tokens_t_psd, bn)
                    act(tokens_t[:, :, :], tokens_t_ps.rearrange("p (c n) -> p c n", c=DC), ACT.Copy)\
                        .then_inc(tokens_t_done, 1)
                if f is not None:
                    act_e.wait_ge(out_ready, fn)
                    act_e.dma_start(out[bass.ds(f * P, out_rows), :], out_blk[0:out_rows, :]).then_inc(out_stored, 16)
                if b is not None:
                    act_e.wait_ge(max_done, bn)
                    act(exps[:, :], logits_ps, ACT.Exp, bias=logit_max[:, :], accum_out=exp_sum[:, :])\
                        .then_inc(exp_done, 1)

            turn(0, None)
            with act_e.Fori(1, NB - 1) as b:
                turn(b, b - 1)
            turn(NB - 1, NB - 2, rows=LAST)
            turn(None, NB - 1, out_rows=LAST)
            act_e.wait_ge(out_stored, 16 * (NB + 1))

        @block.vector
        def _(dve):
            v = nc.vector
            done = [0]

            def link(ins):
                done[0] += 1
                ins.then_inc(dve_chain, 1)
                dve.wait_ge(dve_chain, done[0])

            link(v.memset(x_rest[:, :], 0.0))
            dve.wait_ge(s_edge[1], EDGE_IN)
            dve.wait_ge(fill_done, 3)
            v.tensor_copy(edge_raw[:, 1, :], edge_int[:, 1, :]).then_inc(float_done[1], 1)
            dve.wait_ge(float_done[1], 1)
            rows = edge_raw[:, 1, :].rearrange("p (m f) -> p m f", f=P)
            v.tensor_reduce(tile_lim[:, 0, :], rows, AX, ALU.min).then_inc(lim_done, 1)
            v.tensor_reduce(tile_lim[:, 1, :], rows, AX, ALU.max).then_inc(lim_done, 1)

            def row_stats(g):
                if g < NG:
                    j, n = groups[g]
                    dve.wait_ge(s_x[g], 16)
                    with dve.Fori(j, j + n) as r:
                        v.bn_stats(stats[:, bass.ds(r * 6, 6)], x_all[:, bass.ds(r * D, D)]).then_inc(stats_done, 1)
                    dve.wait_ge(stats_done, j + n)
                    for r in range(j, j + n):
                        v.bn_aggr(mean_var[:, r * 2:r * 2 + 2], stats[:, r * 6:r * 6 + 6]).then_inc(aggr_done, 1)
                    dve.wait_ge(aggr_done, j + n)
                else:
                    j, n = J, 1
                    dve.wait_ge(s_x[NG], 16)
                    v.bn_stats(stats[:, J * 6:J * 6 + 6], x_rest[:, :]).then_inc(stats_done, 1)
                    dve.wait_ge(stats_done, J + 1)
                    v.bn_aggr(mean_var[:, J * 2:J * 2 + 2], stats[:, J * 6:J * 6 + 6]).then_inc(aggr_done, 1)
                    dve.wait_ge(aggr_done, J + 1)
                mv = mean_var[:, :].rearrange("p (j t) -> p j t", t=2)
                v.tensor_scalar_add(var_eps[:, j:j + n], mv[:, j:j + n, 1], LN_EPS).then_inc(var_done, 1)

            def row_scale(g):
                j, n = (groups + [(J, 1)])[g]
                mv = mean_var[:, :].rearrange("p (j t) -> p j t", t=2)
                dve.wait_ge(std_done, g + 1)
                link(v.reciprocal(rstd_all[:, j:j + n], std[:, j:j + n]))
                v.scalar_tensor_tensor(shift_all[:, j:j + n], mv[:, j:j + n, 0], -1.0, rstd_all[:, j:j + n],
                                       ALU.mult, ALU.mult).then_inc(scale_done, 1)

            def quad_limits():
                dve.wait_ge(lim_t_done, 1)
                for a, op in enumerate((ALU.min, ALU.max)):
                    last = v.tensor_reduce(quad_lim[:, a, :],
                                           bank[0][0:MB, a * P:(a + 1) * P].rearrange("m (q k) -> m q k", k=QUAD),
                                           AX, op)
                    last.then_inc(quad_lim_done, 1)

            def make_table():
                T = lambda c: tab[:, c:c + 1]
                b128 = base[0:NB, :]
                lo, hi, ordered, ulo, uhi, diff = 0, 1, 2, 4, 5, 6
                dve.wait_ge(quad_back, 16)
                dve.wait_ge(consts_done, 7)
                least, most = quad_all[:, 0, 0:NQ], quad_all[:, 1, 0:NQ]
                v.tensor_scalar(scratch_q[:, :], most, b128, None, ALU.is_lt, ALU.add, accum_out=T(lo)).then_inc(dve_chain, 1)
                done[0] += 1
                dve.wait_ge(dve_chain, done[0])
                link(v.tensor_scalar(T(diff), b128, float(P), None, ALU.add))
                link(v.tensor_scalar(scratch_q[:, :], least, T(diff), None, ALU.is_lt, ALU.add, accum_out=T(hi)))
                link(v.tensor_tensor(scratch_q[:, 0:NQ - 1], most[:, 0:NQ - 1], least[:, 1:NQ], ALU.is_le))
                link(v.tensor_reduce(T(ordered), scratch_q[:, 0:NQ - 1], AX, ALU.add))
                link(v.tensor_scalar(T(ordered), T(ordered), float(NQ - 1), None, ALU.is_equal))
                link(v.tensor_scalar(T(lo), T(lo), float(NQ - 1), None, ALU.min))
                link(v.tensor_scalar(T(diff), T(lo), 1.0, None, ALU.add))
                link(v.tensor_tensor(T(hi), T(hi), T(diff), ALU.max))
                link(v.tensor_scalar(T(ulo), b128, float(NQ) / P, None, ALU.mult))
                link(v.tensor_scalar(T(uhi), T(ulo), float(NQ), None, ALU.add))
                for limit, all_ in ((lo, ulo), (hi, uhi)):
                    link(v.tensor_tensor(T(diff), T(limit), T(all_), ALU.subtract))
                    link(v.scalar_tensor_tensor(T(limit), T(diff), T(ordered), T(all_), ALU.mult, ALU.add))
                v.tensor_tensor(T(NVIS), T(hi), T(lo), ALU.subtract).then_inc(nv_done, 1)
                dve.wait_ge(nv_done, 1)
                link(v.tensor_scalar(scratch_q[:, :], quad_no[:, :], T(lo), float(-BACK), ALU.subtract, ALU.add))
                v.tensor_scalar(scratch_q[:, :], scratch_q[:, :], 0.0, T(NVIS), ALU.max, ALU.min)\
                    .then_inc(released_parts, 1)
                link(v.tensor_copy(table_i[:, 0:2], tab[:, 0:2]))

            def end_table():
                T = lambda c: tab[:, c:c + 1]
                lo, ordered, uhi, diff = 0, 2, 5, 6
                dve.wait_ge(vbase_psd, 1)
                link(v.tensor_tensor(T(diff), bank[0][0:NB, 256:257], T(lo), ALU.subtract))
                link(v.tensor_copy(table_i[:, 2:3], T(diff)))
                link(v.tensor_scalar(T(uhi), T(ordered), float(1 - NB), float(NB), ALU.mult, ALU.add))
                v.tensor_copy(table_i[:, 3:4], T(uhi)).then_inc(table_done, 1)
                dve.wait_ge(released_psd, 1)
                v.tensor_scalar_add(released[:, :], bank[3][0:1, 0:NQ], 1.0).then_inc(released_done, 1)

            for g in range(NLN):
                row_stats(g)
                if g == 0:
                    quad_limits()
                if g >= 1:
                    row_scale(g - 1)
                if g == 2:
                    make_table()
                if g == 3:
                    end_table()
            row_scale(NLN - 1)
            if NLN < 3:
                make_table()
            if NLN < 4:
                end_table()
            dve.wait_ge(s_small, 80)
            link(v.tensor_tensor(bias_gnn[:, 0, :], bias_gnn[:, 0, :], bias_gnn[:, 1, :], ALU.add))
            dve.wait_ge(consts_done, 7)
            link(v.tensor_copy(iota_block[:, :], iota_row[:, :]))
            dve.wait_ge(edge_t_done[1], PACKS)
            dve.wait_ge(edge_t_done[2], PACKS)
            dve.wait_ge(table_in, 16)

            def edges(b):
                lo = dve.value_load(table[0:1, bass.ds(b * TABLE, 1)], min_val=0, max_val=NB * NQ - 1)
                hi = dve.value_load(table[0:1, bass.ds(b * TABLE + 1, 1)], min_val=1, max_val=NB * NQ)
                visits = dve.value_load(table[0:1, bass.ds(b * TABLE + 2, 1)], min_val=0, max_val=NB * NQ)
                with dve.Fori(lo, hi) as g:
                    col = dve.snap((g % NQ) * QUAD)
                    visit = dve.snap(g + visits + 1)
                    for k in range(QUAD):
                        dve.wait_ge(onehot_used[k], visit)
                        v.tensor_scalar(onehot[k][:, :], iota_block[:, :], dst_t[:, bass.ds(col + k, 1)],
                                        wgt_t[:, bass.ds(col + k, 1)], ALU.is_equal, ALU.mult)\
                            .then_inc(onehot_ready[k], 1)

            def turn(b, f):
                bn = None if b is None else dve.snap(b + 1) if not isinstance(b, int) else b + 1
                fn = None if f is None else dve.snap(f + 1) if not isinstance(f, int) else f + 1
                n = [0]
                if b is not None:
                    dve.sem_clear(gnn_chain)

                def then(ins):
                    n[0] += 1
                    ins.then_inc(gnn_chain, 1)
                    dve.wait_ge(gnn_chain, n[0])

                def rsqrt(t, val):
                    y, a, hv = t[:, 0:1], t[:, 1:2], t[:, 2:3]
                    then(v.tensor_scalar(t[:, 3:4].bitcast(i32), val.bitcast(i32), 1, None, ALU.arith_shift_right))
                    then(v.tensor_scalar(y.bitcast(i32), t[:, 3:4].bitcast(i32), -1.0, float(0x5F3759DF),
                                         ALU.mult, ALU.add))
                    then(v.tensor_scalar(hv, val, -0.5, None, ALU.mult))
                    for _ in range(3):
                        then(v.tensor_tensor(a, y, y, ALU.mult))
                        then(v.tensor_scalar(a, a, hv, 1.5, ALU.mult, ALU.add))
                        then(v.tensor_tensor(y, y, a, ALU.mult))

                def add_expert(e):
                    if f is None:
                        return
                    dve.wait_ge(y_done[e], fn)
                    if e:
                        dve.wait_ge(acc_done[e - 1], fn)
                    v.scalar_tensor_tensor(acc[:, :], y_ps[e % 2], combine[:, e:e + 1],
                                           acc[:, :] if e else resid[:, :], ALU.mult, ALU.add)\
                        .then_inc(acc_done[e], 1)

                if b is not None:
                    edges(b)
                    dve.wait_ge(x_loaded, bn * 32)
                    dve.wait_ge(neigh_done, bn)
                    v.scalar_tensor_tensor(mixed[:, :], xn_blk[:, :], 1.0, neigh_ps, ALU.add, ALU.mult)\
                        .then_inc(mixed_done, 1)
                    then(v.tensor_scalar_add(iota_block[:, :], iota_block[:, :], float(P)))
                add_expert(0)
                add_expert(1)
                add_expert(2)
                if b is not None:
                    dve.wait_ge(dense_done, bn)
                    then(v.tensor_tensor(pre[:, :], dense_ps, bias_gnn[:, 0, :], ALU.add))
                    then(v.scalar_tensor_tensor(act[:, :], pre[:, :], LEAKY_SLOPE, pre[:, :], ALU.mult, ALU.max))
                    then(v.scalar_tensor_tensor(junk[:, :], act[:, :], 1.0, act[:, :], ALU.mult, ALU.mult,
                                                accum_out=sumsq[:, :]))
                    then(v.tensor_scalar(sumsq[:, :], sumsq[:, :], NORM_EPS * NORM_EPS, None, ALU.max))
                    rsqrt(newton[0], sumsq[:, :])
                add_expert(3)
                if b is not None:
                    v.scalar_tensor_tensor(x1[:, :], act[:, :], newton[0][:, 0:1], x_blk[:, :], ALU.mult, ALU.add)\
                        .then_inc(x_used, 1)
                    dve.wait_ge(x_used, bn)
                    then(v.bn_stats(st2[:, :], x1[:, :]))
                    then(v.bn_aggr(mv2[:, :], st2[:, :]))
                    then(v.tensor_scalar(sumsq[:, :], mv2[:, 1:2], LN_EPS, None, ALU.add))
                add_expert(4)
                if b is not None:
                    rsqrt(newton[1], sumsq[:, :])
                    v.tensor_scalar(tokens[:, :], x1[:, :], mv2[:, 0:1], newton[1][:, 0:1],
                                    ALU.subtract, ALU.mult).then_inc(tokens_done, 1)
                    dve.wait_ge(tokens_done, bn)
                    then(v.tensor_tensor(resid[:, :], x1[:, :], tokens[:, :], ALU.add))
                add_expert(5)
                add_expert(6)
                add_expert(7)
                if f is not None:
                    dve.wait_ge(acc_done[NE - 1], fn)
                    dve.wait_ge(b2_done, fn)
                    dve.wait_ge(out_stored, fn * 16)
                    v.tensor_tensor(out_blk[:, :], b2_ps, acc[:, :], ALU.add).then_inc(out_ready, 1)
                if b is not None:
                    dve.wait_ge(logits_done, bn)
                    v.tensor_reduce(logit_max[:, :], logits_ps, AX, ALU.max, negate=True).then_inc(max_done, 1)
                    dve.wait_ge(exp_done, bn)
                    then(v.reciprocal(exp_rec[:, :], exp_sum[:, :]))
                    then(v.tensor_scalar(probs[:, :], exps[:, :], exp_rec[:, :], None, ALU.mult))
                    then(v.max(top[:, :], probs[:, :]))
                    then(v.tensor_scalar(den[:, :], top[:, 0:1], top[:, 1:2], 1e-12, ALU.add, ALU.max))
                    then(v.reciprocal(den_rec[:, :], den[:, :]))
                    then(v.max_index(top_at[:, :], top[:, :], probs[:, :]))
                    then(v.tensor_copy(top_f[:, :], top_at[:, 0:2]))
                    then(v.tensor_scalar(mask1[:, :], iota_row[:, 0:NE], top_f[:, 0:1], None, ALU.is_equal))
                    then(v.scalar_tensor_tensor(mask2[:, :], iota_row[:, 0:NE], top_f[:, 1:2], mask1[:, :],
                                                ALU.is_equal, ALU.add))
                    v.scalar_tensor_tensor(combine[:, :], probs[:, :], den_rec[:, :], mask2[:, :],
                                           ALU.mult, ALU.mult).then_inc(combine_done, 1)

            turn(0, None)
            with dve.Fori(1, NB) as b:
                turn(b, b - 1)
            turn(None, NB - 1)


_INS = ["x", "src", "dst", "edge_weight", "L0_gnn_W1", "L0_gnn_b1", "L0_gnn_W2", "L0_gnn_b2",
        "L0_ffn_router_w", "L0_ffn_w1", "L0_ffn_b1", "L0_ffn_w2", "L0_ffn_b2"]


def kernel(**inputs):
    import numpy as _np
    import concourse.bacc as _bacc
    from concourse import mybir as _mybir
    from concourse.bass_utils import run_bass_kernel_spmd as _run

    nc = _bacc.Bacc("TRN2", target_bir_lowering=False, num_devices=1)
    arrays, args = {}, []
    for name in _INS:
        a = _np.ascontiguousarray(inputs[name])
        arrays[f"in_{name}_dram"] = a
        args.append(nc.dram_tensor(f"in_{name}_dram", a.shape, _mybir.dt.from_np(a.dtype), kind="ExternalInput").ap())
    shape = inputs["x"].shape
    out = nc.dram_tensor("out_0_dram", shape, _mybir.dt.float32, kind="ExternalOutput").ap()
    gnn_ffn_kernel(nc, *args, out)
    r = _run(nc, [arrays], core_ids=[0])
    return r.results[0]["out_0_dram"]
```
